# Optimizing a Trainium2 kernel written in Bass

```python
import numpy as np
import jax
import jax.numpy as jnp

def _softmax(x, axis=-1):
    return jax.nn.softmax(x, axis=axis)

def _gelu(x):
    return jax.nn.gelu(x, approximate=True)

def _silu(x):
    return jax.nn.silu(x)

def _sigmoid(x):
    return jax.nn.sigmoid(x)

def _layernorm(x, axis=-1, eps=1e-05):
    m = jnp.mean(x, axis=axis, keepdims=True)
    v = jnp.var(x, axis=axis, keepdims=True)
    return (x - m) / jnp.sqrt(v + eps)

def _scatter_add(tgt, idx, src, axis=0):
    return tgt.at[idx].add(src)

def _segment_sum(src, seg, n):
    return jax.ops.segment_sum(src, seg, n)
kernel_name = 'mk_cond_resid_d2_seqx_r2_bfb44b'

def setup_inputs(seed: int=0):
    np.random.seed(seed)
    _w = jnp.asarray

    def _rec_inputs():
        import jax
        import jax.numpy as jnp
        _rk = jax.random.key(seed)
        x = 7.22e-05 + 1 * jax.random.normal(jax.random.fold_in(_rk, 1), (16, 512, 1024), jnp.float32)
        _lenS = 512 - jax.random.randint(jax.random.fold_in(_rk, 7), (16,), 0, max(1, 512 // 4) + 1, jnp.int32)
        _lenS2 = 512 - jax.random.randint(jax.random.fold_in(_rk, 8), (16,), 0, max(1, 512 // 4) + 1, jnp.int32)
        cond_2048 = jax.random.bernoulli(jax.random.fold_in(_rk, 11), 0.5063, (16, 1024)).astype(jnp.float32)
        return (x, cond_2048)
    x, cond_2048 = _rec_inputs()

    def _L0_cond_setup():
        import jax, jax.numpy as jnp
        import numpy as np
        NH = 8
        NEG = -1e+30
        key = jax.random.key(seed)
        k1, k2, k3, k4 = jax.random.split(key, 4)
        B, D, T = (4, 512, 1024)
        x = jax.random.normal(k1, (B, D, T), dtype=jnp.float32)
        mask = jax.random.randint(k2, (B, T), 0, 2).astype(jnp.float32)
        lim = float(np.sqrt(6.0 / (D + D)))
        Wq = jax.random.uniform(k3, (D, D), dtype=jnp.float32, minval=-lim, maxval=lim)
        Wo = jax.random.uniform(k4, (D, D), dtype=jnp.float32, minval=-lim, maxval=lim)
        return {'x': x, 'mask': mask, 'Wq': Wq, 'Wo': Wo}
    _L0_cond_all = _L0_cond_setup()
    _L0_cond_in = {k: v for k, v in _L0_cond_all.items() if k in ('Wq', 'Wo')}
    del _L0_cond_all

    def _L1_cond_setup():
        import jax, jax.numpy as jnp
        import numpy as np
        key = jax.random.key(seed)
        k1, k2, k3 = jax.random.split(key, 3)
        B, L, D, K = (4, 2048, 1024, 4)
        x = jax.random.normal(k1, (B, L, D), dtype=jnp.float32)
        w = jax.random.normal(k2, (K, 1, D), dtype=jnp.float32) * 0.1
        b = jax.random.normal(k3, (D,), dtype=jnp.float32) * 0.1
        return {'x': x, 'w': w, 'b': b}
    _L1_cond_all = _L1_cond_setup()
    _L1_cond_in = {k: v for k, v in _L1_cond_all.items() if k in ('b',)}
    del _L1_cond_all
    return {'x': x, 'cond_2048': cond_2048, 'L0_cond_Wq': _L0_cond_in['Wq'], 'L0_cond_Wo': _L0_cond_in['Wo'], 'L1_cond_b': _L1_cond_in['b']}

def reference(x, cond_2048, L0_cond_Wq, L0_cond_Wo, L1_cond_b):
    import jax
    import jax.numpy as jnp

    def _L0_cond_ref(x, mask, Wq, Wo):
        import jax, jax.numpy as jnp
        import numpy as np
        NH = 8
        NEG = -1e+30
        B, D, T = x.shape
        dk = D // NH
        scale = 1.0 / jnp.sqrt(jnp.asarray(dk, x.dtype))
        xt = jnp.transpose(x, (0, 2, 1))
        q = xt @ Wq.T
        qh = q.reshape(B, T, NH, dk).transpose(0, 2, 1, 3)
        scores = scale * jnp.einsum('bhqd,bhkd->bhqk', qh, qh)
        cmask = mask[:, None, None, :]
        rmask = mask[:, None, :, None]
        logits = (scores * cmask + (1.0 - cmask) * NEG) * rmask
        attn = jax.nn.softmax(logits, axis=-1)
        ctx = jnp.einsum('bhqk,bhkd->bhqd', attn, qh)
        ctx = ctx.transpose(0, 2, 1, 3).reshape(B, T, D)
        out = ctx @ Wo.T
        return jnp.transpose(out, (0, 2, 1))

    def _L1_cond_ref(x, w, b):
        import jax, jax.numpy as jnp
        import numpy as np
        'Depthwise causal conv1d, channel-last.\n            x: (B, L, D); w: (K, 1, D); b: (D,). Returns (B, L, D).\n            Matches torch: Conv1d(D, D, K, groups=D, padding=K-1)(x.T)[..., :L].T\n            which is exactly a causal conv (left pad K-1, trim to L).\n            '
        K = w.shape[0]
        D = x.shape[-1]
        y = jax.lax.conv_general_dilated(x, w, window_strides=(1,), padding=[(K - 1, 0)], feature_group_count=D, dimension_numbers=('NWC', 'WIO', 'NWC'))
        return y + b
    x = x + _L0_cond_ref(x, cond_2048, L0_cond_Wq, L0_cond_Wo)
    x = x + _L1_cond_ref(x, cond_2048[:, None, :], L1_cond_b)
    return x

_drawn_inputs = setup_inputs


def setup_inputs(seed=0):
    import zlib

    import numpy as np

    out = dict(_drawn_inputs(seed))
    spreads = {}
    factors = {}
    for name, (base, spread) in spreads.items():
        noise = np.random.default_rng([zlib.crc32(name.encode()), seed]).standard_normal(out[name].shape)
        drawn = base * np.exp(spread * noise) if base else spread * noise
        out[name] = jnp.asarray(drawn.astype(out[name].dtype))
    for name, factor in factors.items():
        out[name] = (out[name] * factor).astype(out[name].dtype)
    return out
```

```python
import numpy as np

import concourse.bass as bass
from concourse import mybir
from contextlib import ExitStack

F32 = mybir.dt.float32
F32R = mybir.dt.float32r
BF16 = mybir.dt.bfloat16
ACT = mybir.ActivationFunctionType
ALU = mybir.AluOpType
AX = mybir.AxisListType

B, D, T = 16, 512, 1024
NH, DK = 8, 64
P = 128
HALF = 512
PAIRS = NH // 2
DT = D // P
KT = T // P
SCALE = DK ** -0.5
BIG = 1e30
BAND = 96
NP32, NPHI, NPLO = 4, 4, 2
LAG = 2

MAX_AT = {1: [0], 2: [1], 3: [2, 3], 4: [4], 5: [5, 6], 6: [7]}
VT_AT = {3: 0, 5: 1}
PROJ_AT = {2: 0, 4: 1}
OUT_AT = {(0, 1, 0): 0, (0, 1, 2): 1, (0, 1, 4): 2, (0, 1, 6): 3,
          (1, 0, 0): 4, (1, 0, 1): 5, (1, 0, 6): 6, (1, 0, 7): 7}


def misc_items(p, i, t, first_pair, out_prev, has_next_pair, has_next_head):
    items = []
    if i == 0 and t == 3 and not first_pair:
        items += [("den", 0), ("den", 1)]
    if has_next_head:
        for q in MAX_AT.get(t, []):
            items += [("max", q, 0), ("max", q, 1)]
        if t in VT_AT:
            items.append(("vt", VT_AT[t]))
    if i == 0 and t in PROJ_AT and has_next_pair:
        items.append(("proj", PROJ_AT[t]))
    if out_prev and (p, i, t) in OUT_AT:
        items.append(("out", OUT_AT[(p, i, t)]))
    if has_next_head and t == 7:
        items.append(("mt",))
    return items


def batch_items(first, last):
    steps = {}
    for p in range(PAIRS):
        for i in range(2):
            for t in range(KT):
                end = last and p == PAIRS - 1
                steps[(p, i, t)] = misc_items(p, i, t, first and p == 0, not first, not end, not (end and i == 1))
    return steps


HEAD_START = [("max", q, h) for q in range(KT) for h in range(2)] + [("vt", 0), ("vt", 1), ("mt",)]
PHASES = {
    "start": {"pair": [("proj", 0), ("proj", 1)], "head": HEAD_START},
    "first": batch_items(True, False),
    "mid": batch_items(False, False),
    "last": batch_items(False, True),
    "end": {"den": [("den", 0), ("den", 1)], "out": [("out", o) for o in range(2 * DT)]},
}
PER_BATCH = sum(len(x) for x in PHASES["mid"].values())
assert PER_BATCH % 2 == 0


def bank_uses():
    at, n = {}, 0
    for phase, steps in PHASES.items():
        for step, items in steps.items():
            for item in items:
                at[(phase, step, item)] = n
                n += 1
        if phase == "mid":
            n += PER_BATCH * (B - 3)
    return at


USES = bank_uses()


def build_attention(nc, x, cond, wqT, woT, x1):
    with ExitStack() as ctx:
        def sb(name, shape, dt):
            return ctx.enter_context(nc.sbuf_tensor(name, shape, dt))

        def ps(name, shape):
            return ctx.enter_context(nc.psum_tensor(name, shape, F32))

        def sem(name):
            return ctx.enter_context(nc.semaphore(name))

        wq = sb("wq", [P, DT, D], F32)
        wo = sb("wo", [P, PAIRS, D], F32)
        ident = sb("ident", [P, P], F32)
        ident_r = sb("ident_r", [P, P], F32R)
        pick = sb("pick", [P, 2, P], F32)
        xb = sb("xb", [P, DT, T], F32)
        mask = sb("mask", [P, T], F32)
        mask8 = sb("mask8", [KT, P], F32)
        off8 = sb("off8", [KT, P], F32R)
        hi = sb("hi", [P, T], F32R)
        lo = sb("lo", [P, T], F32R)
        mhi = sb("mhi", [P, T], F32R)
        mlo = sb("mlo", [P, T], F32R)
        keys = sb("keys", [P, 2, T], F32R)
        quer = sb("quer", [P, 2, T], F32R)
        keys2 = sb("keys2", [BAND, 2, T], F32R)
        quer2 = sb("quer2", [BAND, 2, T], F32R)
        val = sb("val", [P, 2, KT, P], F32R)
        mx = sb("mx", [P, 2 * KT], F32)
        mrow = sb("mrow", [P, KT], F32)
        mneg = sb("mneg", [KT, P], F32)
        mparts = sb("mparts", [KT, 3, P], F32R)
        p32 = sb("p32", [P, NP32, T], F32)
        phi = sb("phi", [P, NPHI, T], F32R)
        plo = sb("plo", [P, NPLO, T], F32R)
        psumk = sb("psumk", [P, 4, T], F32)
        ca = sb("ca", [P, T], F32)
        cb = sb("cb", [P, T], F32)
        rden = sb("rden", [P, T], F32)
        cnorm = sb("cnorm", [P, T], F32)
        ct = sb("ct", [P, PAIRS, T], F32)
        xo = sb("xo", [P, 2, T], F32)

        sc = ps("sc", [P, 2, T])
        pv = ps("pv", [P, T])
        misc = ps("misc", [P, 2, HALF])

        s_const = sem("s_const")
        s_ident = sem("s_ident")
        s_x = sem("s_x")
        s_mask8 = sem("s_mask8")
        s_off8 = sem("s_off8")
        bank_full = [sem("bank_full0"), sem("bank_full1")]
        bank_free = [sem("bank_free0"), sem("bank_free1")]
        s_hi = sem("s_hi")
        s_lo = sem("s_lo")
        s_masked = sem("s_masked")
        s_ops = [sem("s_ops0"), sem("s_ops1")]
        s_rows = [sem("s_rows0"), sem("s_rows1")]
        s_zero = sem("s_zero")
        s_val = sem("s_val")
        s_mx = sem("s_mx")
        s_mrow = sem("s_mrow")
        s_mneg = sem("s_mneg")
        s_mphi = sem("s_mphi")
        s_mparts = sem("s_mparts")
        s_sc = sem("s_sc")
        s_p32 = sem("s_p32")
        s_phi = sem("s_phi")
        s_plo = sem("s_plo")
        s_sum = sem("s_sum")
        s_pv = sem("s_pv")
        s_cab = sem("s_cab")
        s_rden = sem("s_rden")
        s_cadd = sem("s_cadd")
        s_cnorm = sem("s_cnorm")
        s_ct = sem("s_ct")
        s_xo_in = [sem("s_xo_in0"), sem("s_xo_in1")]
        s_xo = sem("s_xo")
        s_xo_out = [sem("s_xo_out0"), sem("s_xo_out1")]

        def head(b, p, i):
            return b * NH + 2 * p + i

        def pair(b, p):
            return b * PAIRS + p

        def bank(phase, b, step, item):
            n = USES[(phase, step, item)]
            if phase == "mid":
                return n % 2, n // 2 + (b - 1) * (PER_BATCH // 2)
            return n % 2, n // 2

        def following(b, p, i):
            if i == 0:
                return b, p, 1
            return (b, p + 1, 0) if p < PAIRS - 1 else (b + 1, 0, 0)

        def next_pair(b, p):
            return (b, p + 1) if p < PAIRS - 1 else (b + 1, 0)

        def before(b, p):
            return (b, p - 1) if p > 0 else (b - 1, PAIRS - 1)

        def run(eng, start, batch, end):
            start()
            batch("first", 0)
            with eng.Fori(1, B - 1) as b:
                batch("mid", b)
            batch("last", B - 1)
            end()

        def half(h):
            return slice(h * HALF, (h + 1) * HALF)

        def tok(t):
            return slice(t * P, (t + 1) * P)

        x_v = x.rearrange("b (k p) t -> b p k t", p=P)
        cond_v = cond.rearrange("b (o t) -> b o t", o=1)
        block = ctx.enter_context(nc.Block())

        @block.sync
        def _(sp):
            def load_x(b, staged):
                if staged is not None:
                    sp.wait_ge(s_masked, staged)
                sp.dma_start(xb[:], x_v[b]).then_inc(s_x, 16)
                sp.dma_start(mask[:], cond_v[b].to_broadcast([P, T])).then_inc(s_x, 16)

            def load_mask8(b, used):
                if used is not None:
                    sp.wait_ge(s_mparts, used)
                sp.dma_start(mask8[:], cond[b].rearrange("(k n) -> k n", n=P)).then_inc(s_mask8, 16)

            def operands(b, p, i, free):
                if free is not None:
                    sp.wait_ge(s_sc, free)
                sp.wait_ge(s_masked, 2 * pair(b, p) + 2)
                src = slice(DK * i, DK * i + DK)
                for dst, part in ((keys[0:DK, i, :], hi), (keys[DK:P, i, :], lo), (quer[0:DK, i, :], mhi),
                                  (quer[DK:P, i, :], mhi), (keys2[0:DK, i, :], hi), (quer2[0:DK, i, :], mlo)):
                    sp.dma_start(dst.bitcast(F32), part[src, :].bitcast(F32)).then_inc(s_ops[i], 16)

            def rows(b, p, i):
                sp.wait_ge(s_mparts, head(b, p, i) + 1)
                for r in range(3):
                    sp.dma_start(quer2[DK + r:DK + r + 1, i, :].bitcast(F32),
                                 mparts[:, r, :].bitcast(F32)).then_inc(s_rows[i], 16)
                sp.dma_start(keys2[DK + 2:DK + 3, i, :].bitcast(F32), off8[:].bitcast(F32)).then_inc(s_rows[i], 16)

            def context(b, p):
                sp.wait_ge(s_cnorm, pair(b, p) + 1)
                sp.dma_start(ct[:, p, :], cnorm[:]).then_inc(s_ct, 16)

            def load_xo(b, m, wait):
                if wait:
                    sp.wait_ge(s_xo_out[m % 2], b * 32 + 16 * (m // 2))
                sp.dma_start(xo[:, m % 2, :], x_v[b][:, m, :]).then_inc(s_xo_in[m % 2], 16)

            def store_xo(b, m):
                sp.wait_ge(s_xo, b * 2 * DT + 2 * m + 2)
                sp.dma_start(x1[b].rearrange("(k p) t -> k p t", p=P)[m], xo[:, m % 2, :]).then_inc(s_xo_out[m % 2], 16)

            def start():
                sp.dma_start(wq[:], wqT.rearrange("(k p) e -> p k e", p=P)).then_inc(s_const, 16)
                load_x(0, None)
                load_mask8(0, None)
                sp.dma_start(wo[:], woT.rearrange("(k p) e -> p k e", p=P)).then_inc(s_const, 16)
                operands(0, 0, 0, None)
                sp.wait_ge(s_zero, 3)
                rows(0, 0, 0)

            def batch(phase, b):
                for p in range(PAIRS):
                    for i in range(2):
                        end = phase == "last" and p == PAIRS - 1
                        nb, np_, ni = following(b, p, i)
                        if not (end and i == 1):
                            first = phase == "first" and p == 0 and i == 0
                            operands(nb, np_, ni, None if first else head(b, p, i) * KT)
                        if i == 1 and p > 0:
                            context(b, p - 1)
                        if phase != "first" and (p, i) == (0, 0):
                            load_xo(b - 1, 0, True)
                            load_xo(b - 1, 1, True)
                            context(b - 1, PAIRS - 1)
                        if phase != "first" and (p, i) == (0, 1):
                            store_xo(b - 1, 0)
                            store_xo(b - 1, 1)
                        if phase != "last" and (p, i) == (2, 1):
                            load_x(b + 1, 2 * pair(b, 3) + 2)
                        if not (end and i == 1):
                            rows(nb, np_, ni)
                        if phase != "first" and (p, i) == (0, 1):
                            load_xo(b - 1, 2, True)
                            load_xo(b - 1, 3, True)
                        if phase != "first" and (p, i) == (1, 0):
                            store_xo(b - 1, 2)
                            store_xo(b - 1, 3)
                        if phase != "last" and (p, i) == (3, 0):
                            load_mask8(b + 1, head(b, 3, 1) + 1)

            def end():
                load_xo(B - 1, 0, True)
                load_xo(B - 1, 1, True)
                context(B - 1, PAIRS - 1)
                store_xo(B - 1, 0)
                load_xo(B - 1, 2, True)
                store_xo(B - 1, 1)
                load_xo(B - 1, 3, True)
                store_xo(B - 1, 2)
                store_xo(B - 1, 3)
                for s in s_xo_out:
                    sp.wait_ge(s, 32 * B)

            run(sp, start, batch, end)

        @block.tensor
        def _(pe):
            def take(phase, b, step, item):
                k, n = bank(phase, b, step, item)
                if not isinstance(n, int) or n > 0:
                    pe.wait_ge(bank_free[k], n)
                return misc[:, k, :], bank_full[k]

            def project(phase, b, p, step, h):
                out, full = take(phase, b, step, ("proj", h))
                nb, np_ = (b, p) if phase == "start" else next_pair(b, p)
                if h == 0 and np_ == 0:
                    pe.wait_ge(s_x, 32 * nb + 32)
                for k in range(DT):
                    last = pe.matmul(out, wq[:, k, np_ * P:(np_ + 1) * P], xb[:, k, half(h)],
                                     start=(k == 0), stop=(k == DT - 1))
                last.then_inc(full, 1)

            def ops_ready(b, p, i):
                pe.wait_ge(s_ops[i], 96 * (pair(b, p) + 1))

            def maxima(phase, b, step, item, nxt):
                out, full = take(phase, b, step, item)
                _, q, h = item
                if q == 0 and h == 0:
                    ops_ready(*nxt)
                i = nxt[2]
                pe.matmul(out, keys[:, i, tok(q)], quer[:, i, half(h)], start=True, stop=True).then_inc(full, 1)

            def values(phase, b, step, item, nxt):
                out, full = take(phase, b, step, item)
                for k in range(4):
                    last = pe.transpose(out[:, tok(k)].bitcast(F32R), keys[:, nxt[2], tok(4 * item[1] + k)], ident_r[:])
                last.then_inc(full, 1)

            def max_rows(phase, b, step, item, nxt):
                out, full = take(phase, b, step, item)
                pe.wait_ge(s_mrow, head(*nxt) + 1)
                pe.transpose(out[0:KT, 0:P], mrow[:], ident[:]).then_inc(full, 1)

            def denominators(phase, b, step, item, prev):
                out, full = take(phase, b, step, item)
                pe.wait_ge(s_sum, 7 * (head(*prev, 1) + 1))
                for i in range(2):
                    last = pe.matmul(out, pick[:, i, :], psumk[:, 2 * (prev[1] % 2) + i, half(item[1])],
                                     start=(i == 0), stop=(i == 1))
                last.then_inc(full, 1)

            def out_project(phase, b, step, item, prev_b):
                out, full = take(phase, b, step, item)
                m, h = item[1] // 2, item[1] % 2
                if item[1] == 0:
                    pe.wait_ge(s_ct, 64 * (prev_b + 1))
                for k in range(PAIRS):
                    last = pe.matmul(out, wo[:, k, m * P:(m + 1) * P], ct[:, k, half(h)],
                                     start=(k == 0), stop=(k == PAIRS - 1))
                last.then_inc(full, 1)

            def scores(b, p, i, t, first):
                n = head(b, p, i) * KT + t
                if not (first and t < 2):
                    pe.wait_ge(s_phi, n - 1)
                if t == 0:
                    pe.wait_ge(s_rows[i], 64 * (pair(b, p) + 1))
                for h in range(2):
                    pe.matmul(sc[:, t % 2, half(h)], keys[:, i, tok(t)], quer[:, i, half(h)], start=True, stop=False)
                    last = pe.matmul(sc[:, t % 2, half(h)], keys2[:, i, tok(t)], quer2[:, i, half(h)],
                                     start=False, stop=True)
                last.then_inc(s_sc, 1)

            def context(b, p, i, t, first):
                n = head(b, p, i) * KT + t
                if t == 0:
                    pe.wait_ge(s_val, 2 * head(b, p, i) + 2)
                    if not first:
                        pe.wait_ge(s_cab, head(b, p, i))
                pe.wait_ge(s_phi, n + 1)
                pe.wait_ge(s_plo, n + 1)
                for h in range(2):
                    pe.matmul(pv[:, half(h)], val[:, i, t, :], phi[:, t % NPHI, half(h)], start=(t == 0), stop=False)
                    last = pe.matmul(pv[:, half(h)], val[:, i, t, :], plo[:, t % NPLO, half(h)],
                                     start=False, stop=(t == KT - 1))
                last.then_inc(s_pv, 1)

            def do(phase, b, p, step, items, nxt):
                for item in items:
                    if item[0] == "proj":
                        project(phase, b, p, step, item[1])
                    elif item[0] == "max":
                        maxima(phase, b, step, item, nxt)
                    elif item[0] == "vt":
                        values(phase, b, step, item, nxt)
                    elif item[0] == "mt":
                        max_rows(phase, b, step, item, nxt)
                    elif item[0] == "den":
                        denominators(phase, b, step, item, before(b, p))
                    elif item[0] == "out":
                        out_project(phase, b, step, item, b - 1)

            def start():
                pe.wait_ge(s_const, 32)
                pe.wait_ge(s_ident, 4)
                do("start", 0, 0, "pair", PHASES["start"]["pair"], None)
                do("start", 0, 0, "head", PHASES["start"]["head"], (0, 0, 0))

            def batch(phase, b):
                for p in range(PAIRS):
                    for i in range(2):
                        for t in range(KT):
                            first = phase == "first" and p == 0 and i == 0
                            scores(b, p, i, t, first)

                            def lagging():
                                if t >= LAG:
                                    context(b, p, i, t - LAG, first)
                                elif not first:
                                    hb, hp, hi_ = (b, p, 0) if i == 1 else (*before(b, p), 1)
                                    context(hb, hp, hi_, KT + t - LAG, False)
                            if t != LAG:
                                lagging()
                            do(phase, b, p, (p, i, t), PHASES[phase][(p, i, t)], following(b, p, i))
                            if t == LAG:
                                lagging()

            def end():
                for t in range(KT - LAG, KT):
                    context(B - 1, PAIRS - 1, 1, t, False)
                for item in PHASES["end"]["den"]:
                    denominators("end", B - 1, "den", item, (B - 1, PAIRS - 1))
                for item in PHASES["end"]["out"]:
                    out_project("end", B - 1, "out", item, B - 1)

            run(pe, start, batch, end)

        @block.scalar
        def _(act):
            def high_part(phase, b, p, step, h):
                k, n = bank(phase, b, step, ("proj", h))
                nb, np_ = (b, p) if phase == "start" else next_pair(b, p)
                act.wait_ge(bank_full[k], n + 1)
                if h == 0 and phase != "start":
                    for s in s_ops:
                        act.wait_ge(s, 96 * pair(nb, np_))
                act.activation(hi[:, half(h)], misc[:, k, :], ACT.Copy).then_inc(s_hi, 1)

            def values(phase, b, step, item, nxt):
                k, n = bank(phase, b, step, item)
                act.wait_ge(bank_full[k], n + 1)
                if phase != "start" and not (phase == "first" and step[0] == 0 and step[1] == 0):
                    act.wait_ge(s_pv, (head(*nxt) - 1) * KT)
                act.activation(val[:, nxt[2], 4 * item[1]:4 * item[1] + 4, :],
                               misc[:, k, :].rearrange("p (k n) -> p k n", n=P), ACT.Copy).then_inc(s_val, 1)
                act.wait_ge(s_val, 2 * head(*nxt) + item[1] + 1)
                act.sem_inc(bank_free[k], 1)

            def copy_context(b, p, i):
                act.wait_ge(s_pv, (head(b, p, i) + 1) * KT)
                if i == 0 and not (isinstance(b, int) and b == 0 and p == 0):
                    act.wait_ge(s_cnorm, pair(b, p))
                act.activation(ca[DK * i:DK * i + DK, :], pv[0:DK, :], ACT.Copy)
                act.activation(cb[DK * i:DK * i + DK, :], pv[DK:P, :], ACT.Copy).then_inc(s_cab, 1)

            def exponentials(b, p, i, t, first):
                n = head(b, p, i) * KT + t
                act.wait_ge(s_sc, n + 1)
                if not (first and t < NP32):
                    act.wait_ge(s_sum, 7 * head(b, p, i) + (max(t - NP32, 1) if t >= NP32 else t + NP32 - 7))
                    act.wait_ge(s_plo, n - NP32 + 1)
                act.activation(p32[:, t % NP32, :], sc[:, t % 2, :], ACT.Exp, scale=SCALE).then_inc(s_p32, 1)
                if not (first and t < NPHI):
                    act.wait_ge(s_pv, n - NPHI + 1)
                act.activation(phi[:, t % NPHI, :], sc[:, t % 2, :], ACT.Exp, scale=SCALE).then_inc(s_phi, 1)

            def do(phase, b, p, step, items, nxt):
                for item in items:
                    if item[0] == "proj":
                        high_part(phase, b, p, step, item[1])
                    elif item[0] == "vt":
                        values(phase, b, step, item, nxt)

            def start():
                do("start", 0, 0, "pair", PHASES["start"]["pair"], None)
                do("start", 0, 0, "head", PHASES["start"]["head"], (0, 0, 0))

            def batch(phase, b):
                for p in range(PAIRS):
                    for i in range(2):
                        for t in range(KT):
                            first = phase == "first" and p == 0 and i == 0
                            exponentials(b, p, i, t, first)
                            if t == LAG - 1 and not first:
                                copy_context(*((b, p, 0) if i == 1 else (*before(b, p), 1)))
                            do(phase, b, p, (p, i, t), PHASES[phase][(p, i, t)], following(b, p, i))

            def end():
                copy_context(B - 1, PAIRS - 1, 1)

            run(act, start, batch, end)

        @block.gpsimd
        def _(pool):
            def constants():
                pool.memset(ident[:], 0.0).then_inc(s_ident, 1)
                pool.memset(pick[:], 0.0).then_inc(s_ident, 1)
                pool.wait_ge(s_ident, 2)
                pool.affine_select(out=ident[:], in_=ident[:], compare_op=ALU.not_equal, fill=1.0, base=0,
                                   pattern=[[-1, P]], channel_multiplier=1).then_inc(s_ident, 1)
                for i in range(2):
                    pool.memset(pick[:, i, DK * i:DK * i + DK], 1.0)
                pool.wait_ge(s_ident, 3)
                pool.tensor_copy(ident_r[:], ident[:]).then_inc(s_ident, 1)

            def add(b, p, i, t, first):
                n = head(b, p, i) * KT + t
                acc = psumk[:, 2 * (p % 2) + i, :]
                pool.wait_ge(s_p32, n + 1)
                if t == 1:
                    if not (isinstance(b, int) and b == 0 and p < 2):
                        pool.wait_ge(s_rden, 2 * (pair(b, p) - 1))
                    pool.tensor_tensor(acc, p32[:, 0, :], p32[:, 1, :], ALU.add).then_inc(s_sum, 1)
                else:
                    pool.wait_ge(s_sum, 7 * head(b, p, i) + t - 1)
                    pool.tensor_tensor(acc, acc, p32[:, t % NP32, :], ALU.add).then_inc(s_sum, 1)

            def batch(phase, b):
                for p in range(PAIRS):
                    for i in range(2):
                        for t in range(1, KT):
                            add(b, p, i, t, phase == "first" and p == 0 and i == 0)

            run(pool, constants, batch, lambda: None)

        @block.vector
        def _(dve):
            def constants():
                dve.memset(keys2[DK:BAND, :, :].bitcast(F32), 0.0).then_inc(s_zero, 1)
                dve.memset(quer2[DK:BAND, :, :].bitcast(F32), 0.0).then_inc(s_zero, 1)
                dve.wait_ge(s_zero, 2)
                dve.memset(keys2[DK:DK + 2, :, :].bitcast(F32), 1.0).then_inc(s_zero, 1)

            def low_part(phase, b, p, step, h):
                k, n = bank(phase, b, step, ("proj", h))
                nb, np_ = (b, p) if phase == "start" else next_pair(b, p)
                j2 = 2 * pair(nb, np_) + h + 1
                dve.wait_ge(s_hi, j2)
                dve.tensor_tensor(lo[:, half(h)], misc[:, k, :], hi[:, half(h)].bitcast(F32),
                                  ALU.subtract).then_inc(s_lo, 1)
                if h == 0 and np_ == 0:
                    dve.wait_ge(s_x, 32 * nb + 32)
                dve.tensor_tensor(mhi[:, half(h)], hi[:, half(h)].bitcast(F32), mask[:, half(h)], ALU.mult)
                dve.wait_ge(s_lo, j2)
                dve.sem_inc(bank_free[k], 1)
                dve.tensor_tensor(mlo[:, half(h)], lo[:, half(h)].bitcast(F32), mask[:, half(h)],
                                  ALU.mult).then_inc(s_masked, 1)

            def maxima(phase, b, step, item, nxt):
                k, n = bank(phase, b, step, item)
                _, q, h = item
                dve.wait_ge(bank_full[k], n + 1)
                if q == 0 and h == 0 and phase != "start":
                    dve.wait_ge(s_mrow, head(*nxt))
                dve.tensor_reduce(mx[:, 2 * q + h:2 * q + h + 1], misc[:, k, :], AX.X, ALU.max).then_inc(bank_free[k], 1)
                if q == KT - 1 and h == 1:
                    for kk in range(2):
                        m = USES[(phase, step, ("max", q, kk))]
                        base = (b - 1) * (PER_BATCH // 2) if phase == "mid" else 0
                        dve.wait_ge(bank_free[m % 2], m // 2 + 1 + base)
                    if phase != "start":
                        dve.wait_ge(s_mparts, head(*nxt))
                    v = mx[:].rearrange("p (q h) -> p h q", h=2)
                    dve.tensor_tensor(mrow[:], v[:, 0, :], v[:, 1, :], ALU.max).then_inc(s_mrow, 1)

            def max_rows(phase, b, step, item, nxt):
                g = head(*nxt)
                k, n = bank(phase, b, step, item)
                if phase != "start":
                    pb, pp, pi = (nxt[0], nxt[1], 0) if nxt[2] == 1 else (*before(nxt[0], nxt[1]), 1)
                    dve.wait_ge(s_rows[pi], 64 * (pair(pb, pp) + 1))
                if nxt[1] == 0 and nxt[2] == 0:
                    dve.wait_ge(s_mask8, 16 * nxt[0] + 16)
                    dve.tensor_copy(mparts[:, 2, :], mask8[:])
                    dve.tensor_scalar(off8[:], mask8[:], -1.0, BIG, ALU.add, ALU.mult)
                dve.wait_ge(bank_full[k], n + 1)
                dve.scalar_tensor_tensor(out=mneg[:], in0=misc[0:KT, k, 0:P], scalar=-1.0, in1=mask8[:],
                                         op0=ALU.mult, op1=ALU.mult).then_inc(s_mneg, 1)
                dve.wait_ge(s_mneg, g + 1)
                dve.sem_inc(bank_free[k], 1)
                dve.tensor_copy(mparts[:, 0, :], mneg[:]).then_inc(s_mphi, 1)
                dve.wait_ge(s_mphi, g + 1)
                dve.tensor_tensor(mparts[:, 1, :], mneg[:], mparts[:, 0, :].bitcast(F32),
                                  ALU.subtract).then_inc(s_mparts, 1)

            def denominators(phase, b, step, item, prev):
                k, n = bank(phase, b, step, item)
                h = item[1]
                dve.wait_ge(bank_full[k], n + 1)
                j = pair(*prev)
                if h == 0 and not (isinstance(j, int) and j == 0):
                    dve.wait_ge(s_cnorm, j)
                dve.reciprocal(rden[:, half(h)], misc[:, k, :]).then_inc(s_rden, 1)
                dve.wait_ge(s_rden, 2 * j + h + 1)
                dve.sem_inc(bank_free[k], 1)
                if h == 1:
                    dve.wait_ge(s_cab, head(*prev, 1) + 1)
                    dve.tensor_tensor(ca[:], ca[:], cb[:], ALU.add).then_inc(s_cadd, 1)
                    dve.wait_ge(s_cadd, j + 1)
                    if not (isinstance(j, int) and j == 0):
                        dve.wait_ge(s_ct, 16 * j)
                    dve.tensor_tensor(cnorm[:], ca[:], rden[:], ALU.mult).then_inc(s_cnorm, 1)

            def residual(phase, b, step, item, prev_b):
                k, n = bank(phase, b, step, item)
                m, h = item[1] // 2, item[1] % 2
                if h == 0:
                    dve.wait_ge(s_xo_in[m % 2], prev_b * 32 + 16 * (m // 2) + 16)
                dve.wait_ge(bank_full[k], n + 1)
                o = xo[:, m % 2, half(h)]
                dve.tensor_tensor(o, misc[:, k, :], o, ALU.add).then_inc(s_xo, 1)
                dve.wait_ge(s_xo, prev_b * 2 * DT + item[1] + 1)
                dve.sem_inc(bank_free[k], 1)

            def split(b, p, i, t, first):
                n = head(b, p, i) * KT + t
                dve.wait_ge(s_phi, n + 1)
                if not (first and t < NPLO):
                    dve.wait_ge(s_pv, n - NPLO + 1)
                dve.tensor_tensor(plo[:, t % NPLO, :], p32[:, t % NP32, :], phi[:, t % NPHI, :].bitcast(F32),
                                  ALU.subtract).then_inc(s_plo, 1)

            def do(phase, b, p, step, items, nxt):
                for item in items:
                    if item[0] == "proj":
                        low_part(phase, b, p, step, item[1])
                    elif item[0] == "max":
                        maxima(phase, b, step, item, nxt)
                    elif item[0] == "mt":
                        max_rows(phase, b, step, item, nxt)
                    elif item[0] == "den":
                        denominators(phase, b, step, item, before(b, p))
                    elif item[0] == "out":
                        residual(phase, b, step, item, b - 1)

            def start():
                constants()
                do("start", 0, 0, "pair", PHASES["start"]["pair"], None)
                do("start", 0, 0, "head", PHASES["start"]["head"], (0, 0, 0))

            def batch(phase, b):
                for p in range(PAIRS):
                    for i in range(2):
                        for t in range(KT):
                            first = phase == "first" and p == 0 and i == 0
                            if t > 0:
                                split(b, p, i, t - 1, first)
                            elif not first:
                                hb, hp, hh = (b, p, 0) if i == 1 else (*before(b, p), 1)
                                split(hb, hp, hh, KT - 1, False)
                            do(phase, b, p, (p, i, t), PHASES[phase][(p, i, t)], following(b, p, i))

            def end():
                split(B - 1, PAIRS - 1, 1, KT - 1, False)
                for item in PHASES["end"]["den"]:
                    denominators("end", B - 1, "den", item, (B - 1, PAIRS - 1))
                for item in PHASES["end"]["out"]:
                    residual("end", B - 1, "out", item, B - 1)

            run(dve, start, batch, end)


TG = P
CH = 16
NG = P // CH
NC = D // CH
TAPS = B
NB = 2
ROUNDS = B // NB
PER_BANK = HALF // (NB * NC)
FILLS = TG // PER_BANK
NBANK = 8


def build_conv(nc, x1, cond, bias, out):
    with ExitStack() as ctx:
        def sb(name, shape, dt):
            return ctx.enter_context(nc.sbuf_tensor(name, shape, dt))

        def sem(name):
            return ctx.enter_context(nc.semaphore(name))

        toep = sb("toep", [P, 2, TG, P], BF16)
        taps = sb("taps", [P, CH, TG], F32)
        keep = sb("keep", [P, 2, P], F32)
        eye = sb("eye", [P, P], F32)
        own = sb("own", [P, CH], F32)
        brow = sb("brow", [P, TG], F32)
        xin = sb("xin", [P, 2, NB, NC, TG], F32)
        parts = sb("parts", [P, 3, NB, NC, TG], BF16)
        acc = [ctx.enter_context(nc.psum_tensor(f"acc{k}", [P, HALF], F32)) for k in range(NBANK)]

        s_taps = sem("s_taps")
        s_keep = sem("s_keep")
        s_own = sem("s_own")
        s_toep = sem("s_toep")
        s_toep_p = sem("s_toep_p")
        s_in = [sem("s_in0"), sem("s_in1")]
        s_p0 = sem("s_p0")
        s_r0 = sem("s_r0")
        s_p1 = sem("s_p1")
        s_p2 = sem("s_p2")
        s_bank = sem("s_bank")
        s_res = sem("s_res")
        s_out = [sem("s_out0"), sem("s_out1")]
        block = ctx.enter_context(nc.Block())

        def view(t, b, g):
            return t[b, :, g * TG:(g + 1) * TG].rearrange("(c l) n -> l c n", l=CH)

        @block.sync
        def _(sp):
            for l in range(CH):
                for g in range(NG):
                    c = cond[:, g * TG:(g + 1) * TG].rearrange("(o j) n -> o j n", o=1)
                    k = g * CH + l
                    sp.dma_start(taps[k:k + 1, 0:CH - l, :], c[:, l:CH, :]).then_inc(s_taps, 16)
                    if l:
                        sp.dma_start(taps[k:k + 1, CH - l:CH, :], c[:, 0:l, :]).then_inc(s_taps, 16)
            for g in range(NG):
                b = bias[g * TG:(g + 1) * TG].rearrange("(o n) -> o n", o=1)
                sp.dma_start(brow[g * CH:(g + 1) * CH, :], b.to_broadcast([CH, TG])).then_inc(s_taps, 16)

            def load(r, k):
                for j in range(NB):
                    for g in range(NG):
                        sp.dma_start(xin[g * CH:(g + 1) * CH, k, j], view(x1, r * NB + j, g)).then_inc(s_in[k], 16)

            def store(r, k):
                sp.wait_ge(s_res, FILLS * (r + 1))
                for j in range(NB):
                    for g in range(NG):
                        sp.dma_start(view(out, r * NB + j, g), xin[g * CH:(g + 1) * CH, k, j]).then_inc(s_out[k], 16)

            for r in range(2):
                load(r, r)
            for r in range(ROUNDS):
                store(r, r % 2)
                if r + 2 < ROUNDS:
                    sp.wait_ge(s_out[r % 2], 16 * NB * NG * (r // 2 + 1))
                    load(r + 2, r % 2)
            for k in range(2):
                sp.wait_ge(s_out[k], 16 * NB * NG * (ROUNDS // 2))

        N_TAPS = 16 * (NG * (2 * CH - 1) + NG)
        ON_DVE = 11

        @block.gpsimd
        def _(pool):
            pool.memset(keep[:], 1.0).then_inc(s_keep, 1)
            pool.memset(eye[:], 0.0).then_inc(s_keep, 1)
            pool.wait_ge(s_keep, 2)
            m = keep[:, 0, :].rearrange("p (g l) -> p g l", l=CH)
            pool.affine_select(out=m, in_=m, compare_op=ALU.is_ge, fill=0.0, base=0,
                               pattern=[[CH, NG], [1, CH]], channel_multiplier=-1).then_inc(s_keep, 1)
            m1 = keep[:, 1, :].rearrange("p (g l) -> p g l", l=CH)
            pool.affine_select(out=m1, in_=m1, compare_op=ALU.is_ge, fill=0.0, base=-1,
                               pattern=[[-CH, NG], [-1, CH]], channel_multiplier=1).then_inc(s_keep, 1)
            pool.wait_ge(s_keep, 4)
            pool.affine_select(out=m, in_=m, compare_op=ALU.is_ge, fill=0.0, base=0,
                               pattern=[[-CH, NG], [0, CH]], channel_multiplier=1).then_inc(s_keep, 1)
            pool.affine_select(out=m1, in_=m1, compare_op=ALU.is_ge, fill=0.0, base=CH - 1,
                               pattern=[[CH, NG], [0, CH]], channel_multiplier=-1).then_inc(s_keep, 1)
            pool.affine_select(out=eye[:], in_=eye[:], compare_op=ALU.not_equal, fill=1.0, base=0,
                               pattern=[[-1, P]], channel_multiplier=1).then_inc(s_keep, 1)
            pool.wait_ge(s_keep, 7)
            pool.wait_ge(s_taps, N_TAPS)
            for l in range(ON_DVE, CH):
                pool.tensor_tensor(toep[:, 1].rearrange("p n (g l) -> p n g l", l=CH)[:, :, :, l],
                                   taps[:, CH - 1 - l, :].unsqueeze(2).to_broadcast([P, TG, NG]),
                                   keep[:, 1].rearrange("p (o g l) -> p o g l", o=1, l=CH)[:, :, :, l].to_broadcast([P, TG, NG]),
                                   ALU.mult).then_inc(s_toep_p, 1)
            for r in range(ROUNDS):
                pool.wait_ge(s_p0, r + 1)
                x = xin[:, r % 2]
                pool.tensor_tensor(x, x, parts[:, 0], ALU.subtract).then_inc(s_r0, 1)

        @block.scalar
        def _(act):
            for r in range(ROUNDS):
                act.wait_ge(s_in[r % 2], 16 * NB * NG * (r // 2 + 1))
                if r:
                    act.wait_ge(s_bank, FILLS * r)
                act.activation(parts[:, 0], xin[:, r % 2], ACT.Copy).then_inc(s_p0, 1)
                act.wait_ge(s_r0, r + 1)
                act.activation(parts[:, 1], xin[:, r % 2], ACT.Copy).then_inc(s_p1, 1)

        @block.vector
        def _(dve):
            dve.wait_ge(s_keep, 7)
            dve.tensor_reduce(own[:], eye[:].rearrange("p (g l) -> p l g", l=CH), AX.X, ALU.max).then_inc(s_own, 1)
            dve.wait_ge(s_own, 1)
            dve.wait_ge(s_taps, N_TAPS)
            for w in range(2):
                for l in range(CH if w == 0 else ON_DVE):
                    o = toep[:, w].rearrange("p n (g l) -> p n g l", l=CH)[:, :, :, l]
                    c = taps[:, CH - 1 - l, :].unsqueeze(2).to_broadcast([P, TG, NG])
                    m = keep[:, w].rearrange("p (o g l) -> p o g l", o=1, l=CH)[:, :, :, l].to_broadcast([P, TG, NG])
                    if w == 0:
                        dve.scalar_tensor_tensor(out=o, in0=c, scalar=own[:, l:l + 1], in1=m,
                                                 op0=ALU.add, op1=ALU.mult).then_inc(s_toep, 1)
                    else:
                        dve.tensor_tensor(o, c, m, ALU.mult).then_inc(s_toep, 1)
            for r in range(ROUNDS):
                dve.wait_ge(s_p1, r + 1)
                dve.tensor_tensor(parts[:, 2], xin[:, r % 2], parts[:, 1], ALU.subtract).then_inc(s_p2, 1)
                dve.wait_ge(s_p2, r + 1)
                for f in range(FILLS):
                    dve.wait_ge(s_bank, FILLS * r + f + 1)
                    n = slice(f * PER_BANK, (f + 1) * PER_BANK)
                    dve.tensor_tensor(xin[:, r % 2, :, :, n].rearrange("p b c n -> p (b c) n"),
                                      acc[f % NBANK][:].rearrange("p (n k) -> p k n", n=PER_BANK),
                                      brow[:, n].rearrange("p (o n) -> p o n", o=1).to_broadcast([P, NB * NC, PER_BANK]),
                                      ALU.add).then_inc(s_res, 1)

        @block.tensor
        def _(pe):
            pe.wait_ge(s_toep, CH + ON_DVE)
            pe.wait_ge(s_toep_p, CH - ON_DVE)
            for r in range(ROUNDS):
                pe.wait_ge(s_p2, r + 1)
                for f in range(FILLS):
                    if r or f >= NBANK:
                        pe.wait_ge(s_res, FILLS * r + f + 1 - NBANK)
                    for n in range(PER_BANK):
                        tok = f * PER_BANK + n
                        o = acc[f % NBANK][:, n * NB * NC:(n + 1) * NB * NC].rearrange("p (b c) -> p b c", b=NB)
                        for k in range(3):
                            last = pe.matmul(o, toep[:, 0, tok, :], parts[:, k, :, :, tok],
                                             start=(k == 0), stop=False, skip_group_check=True)
                        for k in range(3):
                            last = pe.matmul(o[:, :, 1:NC], toep[:, 1, tok, :], parts[:, k, :, 0:NC - 1, tok],
                                             start=False, stop=(k == 2), skip_group_check=True)
                    last.then_inc(s_bank, 1)


def build(nc, x, cond, wqT, woT, bias, x1, out):
    build_attention(nc, x, cond, wqT, woT, x1)
    build_conv(nc, x1, cond, bias, out)


def kernel(x, cond_2048, L0_cond_Wq, L0_cond_Wo, L1_cond_b):
    import concourse.bacc as bacc
    from concourse.bass_utils import run_bass_kernel_spmd

    nc = bacc.Bacc("TRN2", target_bir_lowering=False, num_devices=1)
    arrays = {
        "x": np.ascontiguousarray(x),
        "cond": np.ascontiguousarray(cond_2048),
        "wqT": np.ascontiguousarray(np.asarray(L0_cond_Wq).T),
        "woT": np.ascontiguousarray(np.asarray(L0_cond_Wo).T),
        "bias": np.ascontiguousarray(L1_cond_b),
    }
    aps = [nc.dram_tensor(k, a.shape, mybir.dt.from_np(a.dtype), kind="ExternalInput").ap() for k, a in arrays.items()]
    x1 = nc.dram_tensor("x1", (B, D, T), F32, kind="Internal").ap()
    out = nc.dram_tensor("out", (B, D, T), F32, kind="ExternalOutput").ap()
    build(nc, *aps, x1, out)
    r = run_bass_kernel_spmd(nc, [arrays], core_ids=[0])
    return r.results[0]["out"]
```

```python
import numpy as np

import concourse.bass as bass
from concourse import mybir
from contextlib import ExitStack

F32 = mybir.dt.float32
F32R = mybir.dt.float32r
BF16 = mybir.dt.bfloat16
ACT = mybir.ActivationFunctionType
ALU = mybir.AluOpType
AX = mybir.AxisListType

B, D, T = 16, 512, 1024
NH, DK = 8, 64
P = 128
HALF = 512
PAIRS = NH // 2
DT = D // P
KT = T // P
SCALE = DK ** -0.5
BIG = 1e30
BAND = 96
NP32, NPHI, NPLO = 4, 4, 2
LAG = 2

MAX_AT = {0: [2], 1: [3], 2: [4], 3: [5], 4: [6, 7]}
MAX_AHEAD_AT = {6: 0, 7: 1}
MT_AT = 5
VT_AT = 6
DCOL_AT = 3
DROW_AT = 4
PROJ_AT = {0: 0, 1: 1}
STAGE_AT = {2: "lo", 3: "mhi", 4: "mlo"}
OUT_AT = {(0, 1, 0): 0, (0, 1, 2): 1, (0, 1, 4): 2, (0, 1, 6): 3,
          (1, 0, 2): 4, (1, 0, 5): 5, (1, 0, 6): 6, (1, 0, 7): 7}


def misc_items(p, i, t, first_pair, out_prev, has_next_pair, has_next_head):
    items = []
    if has_next_head:
        items += [("max", q, 1) for q in MAX_AT.get(t, [])]
    if has_next_pair and t in MAX_AHEAD_AT:
        items.append(("max", MAX_AHEAD_AT[t], 2))
    if t == DCOL_AT and not (first_pair and i == 0):
        items.append(("dcol",))
    if t == DROW_AT and i == 0 and not first_pair:
        items.append(("drow",))
    if has_next_head:
        if t == MT_AT:
            items.append(("mt",))
        if t == VT_AT:
            items.append(("vt",))
    if i == 0 and t in PROJ_AT and has_next_pair:
        items.append(("proj", PROJ_AT[t]))
    if out_prev and (p, i, t) in OUT_AT:
        items.append(("out", OUT_AT[(p, i, t)]))
    return items


def batch_items(first, last):
    steps = {}
    for p in range(PAIRS):
        for i in range(2):
            for t in range(KT):
                end = last and p == PAIRS - 1
                steps[(p, i, t)] = misc_items(p, i, t, first and p == 0, not first, not end, not (end and i == 1))
    return steps


HEAD_START = [("max", q, 0) for q in range(KT)] + [("vt",), ("mt",), ("max", 0, 1), ("max", 1, 1)]
PHASES = {
    "start": {"pair": [("proj", 0), ("proj", 1)], "head": HEAD_START},
    "first": batch_items(True, False),
    "mid": batch_items(False, False),
    "last": batch_items(False, True),
    "end": {"den": [("dcol",), ("drow",)], "out": [("out", o) for o in range(2 * DT)]},
}
PER_BATCH = sum(len(x) for x in PHASES["mid"].values())
assert PER_BATCH % 2 == 0


def bank_uses():
    at, n = {}, 0
    for phase, steps in PHASES.items():
        for step, items in steps.items():
            for item in items:
                at[(phase, step, item)] = n
                n += 1
        if phase == "mid":
            n += PER_BATCH * (B - 3)
    return at


USES = bank_uses()


def build_attention(nc, x, cond, wqT, woT, x1):
    with ExitStack() as ctx:
        def sb(name, shape, dt):
            return ctx.enter_context(nc.sbuf_tensor(name, shape, dt))

        def ps(name, shape):
            return ctx.enter_context(nc.psum_tensor(name, shape, F32))

        def sem(name):
            return ctx.enter_context(nc.semaphore(name))

        wq = sb("wq", [P, DT, D], F32)
        wo = sb("wo", [P, PAIRS, D], F32)
        ident_r = sb("ident_r", [P, P], F32R)
        ident = ident_r[:].bitcast(F32)
        ones = sb("ones", [P, 1], F32)
        xb = sb("xb", [P, DT, T], F32)
        mask = sb("mask", [P, T], F32)
        mask8 = sb("mask8", [KT, P], F32)
        off8 = sb("off8", [KT, P], F32R)
        q32 = sb("q32", [P, T], F32)
        hi = sb("hi", [P, T], F32R)
        lo = sb("lo", [P, T], F32R)
        mhi = sb("mhi", [P, T], F32R)
        mlo = sb("mlo", [P, T], F32R)
        keys = sb("keys", [P, 4, T], F32R)
        quer = sb("quer", [P, 4, T], F32R)
        keys2 = sb("keys2", [BAND, 2, T], F32R)
        quer2 = sb("quer2", [BAND, 2, T], F32R)
        val = sb("val", [P, 2, KT, P], F32R)
        mrow = sb("mrow", [P, KT], F32)
        mneg = sb("mneg", [KT, P], F32)
        mparts = sb("mparts", [KT, 3, P], F32R)
        p32 = sb("p32", [P, NP32, T], F32)
        phi = sb("phi", [P, NPHI, T], F32R)
        plo = sb("plo", [P, NPLO, T], F32R)
        psumk = sb("psumk", [P, 2, T], F32)
        ca = sb("ca", [P, T], F32)
        cb = sb("cb", [P, T], F32)
        rden = sb("rden", [P, 2, KT], F32)
        rwide = cb[:].rearrange("p (k i d) -> p k i d", k=KT, i=2)
        cnorm = sb("cnorm", [P, T], F32)
        ct = sb("ct", [P, PAIRS, T], F32)
        xo = sb("xo", [P, 2, T], F32)

        sc = ps("sc", [P, 2, HALF])
        pv = ps("pv", [P, T])
        misc = ps("misc", [P, 2, T])

        s_const = sem("s_const")
        s_ident = sem("s_ident")
        s_x = sem("s_x")
        s_mask8 = sem("s_mask8")
        s_off8 = sem("s_off8")
        bank_full = [sem("bank_full0"), sem("bank_full1")]
        bank_free = [sem("bank_free0"), sem("bank_free1")]
        s_hi = sem("s_hi")
        s_lo = sem("s_lo")
        s_masked = sem("s_masked")
        s_kq = [sem("s_kq0"), sem("s_kq1")]
        s_kq2 = [sem("s_kq20"), sem("s_kq21")]
        s_rows = [sem("s_rows0"), sem("s_rows1")]
        s_zero = sem("s_zero")
        s_val = sem("s_val")
        s_mrow = sem("s_mrow")
        s_mneg = sem("s_mneg")
        s_mphi = sem("s_mphi")
        s_mparts = sem("s_mparts")
        s_sc = sem("s_sc")
        s_p32 = sem("s_p32")
        s_phi = sem("s_phi")
        s_plo = sem("s_plo")
        s_sum = sem("s_sum")
        s_pv = sem("s_pv")
        s_cab = sem("s_cab")
        s_rden = sem("s_rden")
        s_rwide = sem("s_rwide")
        s_cadd = sem("s_cadd")
        s_cnorm = sem("s_cnorm")
        s_ct = sem("s_ct")
        s_xo_in = [sem("s_xo_in0"), sem("s_xo_in1")]
        s_xo = sem("s_xo")
        s_xo_out = [sem("s_xo_out0"), sem("s_xo_out1")]

        def head(b, p, i):
            return b * NH + 2 * p + i

        def pair(b, p):
            return b * PAIRS + p

        def bank(phase, b, step, item):
            n = USES[(phase, step, item)]
            if phase == "mid":
                return n % 2, n // 2 + (b - 1) * (PER_BATCH // 2)
            return n % 2, n // 2

        def following(b, p, i):
            if i == 0:
                return b, p, 1
            return (b, p + 1, 0) if p < PAIRS - 1 else (b + 1, 0, 0)

        def max_head(phase, item, nxt):
            if phase == "start":
                return (0, 0, item[2])
            return nxt if item[2] == 1 else following(*nxt)

        def next_pair(b, p):
            return (b, p + 1) if p < PAIRS - 1 else (b + 1, 0)

        def before(b, p):
            return (b, p - 1) if p > 0 else (b - 1, PAIRS - 1)

        def head_before(b, p, i):
            return (b, p, 0) if i == 1 else (*before(b, p), 1)

        def run(eng, start, batch, end):
            start()
            batch("first", 0)
            with eng.Fori(1, B - 1) as b:
                batch("mid", b)
            batch("last", B - 1)
            end()

        def half(h):
            return slice(h * HALF, (h + 1) * HALF)

        def tok(t):
            return slice(t * P, (t + 1) * P)

        x_v = x.rearrange("b (k p) t -> b p k t", p=P)
        cond_v = cond.rearrange("b (o t) -> b o t", o=1)
        block = ctx.enter_context(nc.Block())

        @block.sync
        def _(sp):
            def load_x(b, staged):
                if staged is not None:
                    sp.wait_ge(s_masked, staged)
                sp.dma_start(xb[:], x_v[b]).then_inc(s_x, 16)
                sp.dma_start(mask[:], cond_v[b].to_broadcast([P, T])).then_inc(s_x, 16)

            def load_mask8(b, used):
                if used is not None:
                    sp.wait_ge(s_mparts, used)
                sp.dma_start(mask8[:], cond[b].rearrange("(k n) -> k n", n=P)).then_inc(s_mask8, 16)

            def move(dst, part, i):
                return sp.dma_start(dst.bitcast(F32), part[DK * i:DK * i + DK, :].bitcast(F32))

            def operands(b, p):
                sp.wait_ge(s_masked, pair(b, p) + 1)
                for i in range(2):
                    k = 2 * (p % 2) + i
                    for dst, part in ((keys[0:DK, k, :], hi), (keys[DK:P, k, :], lo),
                                      (quer[0:DK, k, :], mhi), (quer[DK:P, k, :], mhi)):
                        move(dst, part, i).then_inc(s_kq[i], 16)

            def operands2(b, p, i, free):
                if free is not None:
                    sp.wait_ge(s_sc, free)
                move(keys2[0:DK, i, :], hi, i).then_inc(s_kq2[i], 16)
                move(quer2[0:DK, i, :], mlo, i).then_inc(s_kq2[i], 16)

            def rows(b, p, i):
                sp.wait_ge(s_mparts, head(b, p, i) + 1)
                for r in range(3):
                    sp.dma_start(quer2[DK + r:DK + r + 1, i, :].bitcast(F32),
                                 mparts[:, r, :].bitcast(F32)).then_inc(s_rows[i], 16)
                sp.dma_start(keys2[DK + 2:DK + 3, i, :].bitcast(F32), off8[:].bitcast(F32)).then_inc(s_rows[i], 16)

            def context(b, p):
                sp.wait_ge(s_cnorm, pair(b, p) + 1)
                sp.dma_start(ct[:, p, :], cnorm[:]).then_inc(s_ct, 16)

            def load_xo(b, m, wait):
                if wait:
                    sp.wait_ge(s_xo_out[m % 2], b * 32 + 16 * (m // 2) + 16)
                sp.dma_start(xo[:, m % 2, :], x_v[b][:, m, :]).then_inc(s_xo_in[m % 2], 16)

            def store_xo(b, m):
                sp.wait_ge(s_xo, b * 2 * DT + 2 * m + 2)
                sp.dma_start(x1[b].rearrange("(k p) t -> k p t", p=P)[m], xo[:, m % 2, :]).then_inc(s_xo_out[m % 2], 16)

            def start():
                for s in s_xo_out:
                    sp.sem_inc(s, 16)
                sp.dma_start(wq[:], wqT.rearrange("(k p) e -> p k e", p=P)).then_inc(s_const, 16)
                load_x(0, None)
                load_mask8(0, None)
                sp.dma_start(wo[:], woT.rearrange("(k p) e -> p k e", p=P)).then_inc(s_const, 16)
                operands(0, 0)
                operands2(0, 0, 0, None)
                sp.wait_ge(s_zero, 3)
                rows(0, 0, 0)

            def batch(phase, b):
                for p in range(PAIRS):
                    for i in range(2):
                        end = phase == "last" and p == PAIRS - 1
                        nb, np_, ni = following(b, p, i)
                        if not (end and i == 1):
                            first = phase == "first" and p == 0 and i == 0
                            operands2(nb, np_, ni, None if first else head(b, p, i) * KT * 2)
                        if i == 1 and p > 0:
                            context(b, p - 1)
                        if phase != "first" and (p, i) == (0, 0):
                            load_xo(b - 1, 0, True)
                            load_xo(b - 1, 1, True)
                            context(b - 1, PAIRS - 1)
                        if phase != "first" and (p, i) == (0, 1):
                            store_xo(b - 1, 0)
                            load_xo(b - 1, 2, True)
                        if phase != "last" and (p, i) == (2, 1):
                            load_x(b + 1, pair(b, 3) + 1)
                        if i == 0 and not end:
                            operands(*next_pair(b, p))
                        if not (end and i == 1):
                            rows(nb, np_, ni)
                        if phase != "first" and (p, i) == (0, 1):
                            store_xo(b - 1, 1)
                            load_xo(b - 1, 3, True)
                        if phase != "first" and (p, i) == (1, 0):
                            store_xo(b - 1, 2)
                            store_xo(b - 1, 3)
                        if phase != "last" and (p, i) == (3, 0):
                            load_mask8(b + 1, head(b, 3, 1) + 1)

            def end():
                load_xo(B - 1, 0, True)
                load_xo(B - 1, 1, True)
                context(B - 1, PAIRS - 1)
                store_xo(B - 1, 0)
                load_xo(B - 1, 2, True)
                store_xo(B - 1, 1)
                load_xo(B - 1, 3, True)
                store_xo(B - 1, 2)
                store_xo(B - 1, 3)
                for s in s_xo_out:
                    sp.wait_ge(s, 32 * B + 16)

            run(sp, start, batch, end)

        @block.tensor
        def _(pe):
            def take(phase, b, step, item):
                k, n = bank(phase, b, step, item)
                if not isinstance(n, int) or n > 0:
                    pe.wait_ge(bank_free[k], n)
                return misc[:, k, :], bank_full[k]

            def project(phase, b, p, step, h):
                out, full = take(phase, b, step, ("proj", h))
                out = out[:, 0:HALF]
                nb, np_ = (b, p) if phase == "start" else next_pair(b, p)
                if h == 0 and np_ == 0:
                    pe.wait_ge(s_x, 32 * nb + 32)
                for k in range(DT):
                    last = pe.matmul(out, wq[:, k, np_ * P:(np_ + 1) * P], xb[:, k, half(h)],
                                     start=(k == 0), stop=(k == DT - 1))
                last.then_inc(full, 1)

            def maxima(phase, b, step, item, nxt):
                nxt = max_head(phase, item, nxt)
                out, full = take(phase, b, step, item)
                q = item[1]
                if q == 0:
                    pe.wait_ge(s_kq[nxt[2]], 64 * (pair(nxt[0], nxt[1]) + 1))
                k = 2 * (nxt[1] % 2) + nxt[2]
                for h in range(2):
                    last = pe.matmul(out[:, half(h)], keys[:, k, tok(q)], quer[:, k, half(h)], start=True, stop=True)
                last.then_inc(full, 1)

            def values(phase, b, step, item, nxt):
                out, full = take(phase, b, step, item)
                for k in range(KT):
                    last = pe.transpose(out[:, tok(k)].bitcast(F32R), keys[:, 2 * (nxt[1] % 2) + nxt[2], tok(k)], ident_r[:])
                last.then_inc(full, 1)

            def max_rows(phase, b, step, item, nxt):
                out, full = take(phase, b, step, item)
                pe.wait_ge(s_mrow, head(*nxt) + 1)
                pe.transpose(out[0:KT, 0:P], mrow[:], ident).then_inc(full, 1)

            def denominators(phase, b, step, item, prev):
                out, full = take(phase, b, step, item)
                pe.wait_ge(s_sum, 7 * (head(*prev) + 1))
                for t in range(KT):
                    last = pe.matmul(out[:, t:t + 1], psumk[:, prev[2], tok(t)], ones[:], start=True, stop=True)
                last.then_inc(full, 1)

            def spread(phase, b, step, item, prev):
                out, full = take(phase, b, step, item)
                pe.wait_ge(s_rwide, pair(*prev) + 1)
                for k in range(KT):
                    r = rwide[:, k, :, :].rearrange("p i d -> p (i d)")
                    last = pe.matmul(out[:, tok(k)], r, ident, start=True, stop=True)
                last.then_inc(full, 1)

            def out_project(phase, b, step, item, prev_b):
                out, full = take(phase, b, step, item)
                out = out[:, 0:HALF]
                m, h = item[1] // 2, item[1] % 2
                if item[1] == 0:
                    pe.wait_ge(s_ct, 64 * (prev_b + 1))
                for k in range(PAIRS):
                    last = pe.matmul(out, wo[:, k, m * P:(m + 1) * P], ct[:, k, half(h)],
                                     start=(k == 0), stop=(k == PAIRS - 1))
                last.then_inc(full, 1)

            def scores(b, p, i, t, first):
                n = head(b, p, i) * KT + t
                k = 2 * (p % 2) + i
                if t == 0:
                    pe.wait_ge(s_kq2[i], 32 * (pair(b, p) + 1))
                    pe.wait_ge(s_rows[i], 64 * (pair(b, p) + 1))
                for h in range(2):
                    if not (first and t == 0):
                        pe.wait_ge(s_phi, 2 * n - 1 + h)
                    pe.matmul(sc[:, h, :], keys[:, k, tok(t)], quer[:, k, half(h)], start=True, stop=False)
                    pe.matmul(sc[:, h, :], keys2[:, i, tok(t)], quer2[:, i, half(h)],
                              start=False, stop=True).then_inc(s_sc, 1)

            def context(b, p, i, t, first):
                n = head(b, p, i) * KT + t
                if t == 0:
                    pe.wait_ge(s_val, head(b, p, i) + 1)
                    if not first:
                        pe.wait_ge(s_cab, head(b, p, i))
                pe.wait_ge(s_phi, 2 * n + 2)
                pe.wait_ge(s_plo, n + 1)
                for h in range(2):
                    pe.matmul(pv[:, half(h)], val[:, i, t, :], phi[:, t % NPHI, half(h)], start=(t == 0), stop=False)
                    last = pe.matmul(pv[:, half(h)], val[:, i, t, :], plo[:, t % NPLO, half(h)],
                                     start=False, stop=(t == KT - 1))
                last.then_inc(s_pv, 1)

            def do(phase, b, p, step, items, nxt):
                for item in items:
                    if item[0] == "proj":
                        project(phase, b, p, step, item[1])
                    elif item[0] == "max":
                        maxima(phase, b, step, item, nxt)
                    elif item[0] == "vt":
                        values(phase, b, step, item, nxt)
                    elif item[0] == "mt":
                        max_rows(phase, b, step, item, nxt)
                    elif item[0] == "dcol":
                        denominators(phase, b, step, item, head_before(b, p, step[1]))
                    elif item[0] == "drow":
                        spread(phase, b, step, item, before(b, p))
                    elif item[0] == "out":
                        out_project(phase, b, step, item, b - 1)

            def start():
                pe.wait_ge(s_const, 32)
                pe.wait_ge(s_ident, 4)
                do("start", 0, 0, "pair", PHASES["start"]["pair"], None)
                do("start", 0, 0, "head", PHASES["start"]["head"], (0, 0, 0))

            def batch(phase, b):
                for p in range(PAIRS):
                    for i in range(2):
                        for t in range(KT):
                            first = phase == "first" and p == 0 and i == 0
                            scores(b, p, i, t, first)

                            def lagging():
                                if t >= LAG:
                                    context(b, p, i, t - LAG, first)
                                elif not first:
                                    hb, hp, hi_ = (b, p, 0) if i == 1 else (*before(b, p), 1)
                                    context(hb, hp, hi_, KT + t - LAG, False)
                            items = PHASES[phase][(p, i, t)]
                            early = [x for x in items if x[0] == "max"]
                            do(phase, b, p, (p, i, t), early, following(b, p, i))
                            if t != LAG:
                                lagging()
                            do(phase, b, p, (p, i, t), items[len(early):], following(b, p, i))
                            if t == LAG:
                                lagging()

            def end():
                for t in range(KT - LAG, KT):
                    context(B - 1, PAIRS - 1, 1, t, False)
                denominators("end", B - 1, "den", ("dcol",), (B - 1, PAIRS - 1, 1))
                spread("end", B - 1, "den", ("drow",), (B - 1, PAIRS - 1))
                for item in PHASES["end"]["out"]:
                    out_project("end", B - 1, "out", item, B - 1)

            run(pe, start, batch, end)

        @block.scalar
        def _(act):
            def high_part(phase, b, p, step, h):
                k, n = bank(phase, b, step, ("proj", h))
                nb, np_ = (b, p) if phase == "start" else next_pair(b, p)
                act.wait_ge(bank_full[k], n + 1)
                if h == 0 and phase != "start":
                    for i in range(2):
                        act.wait_ge(s_kq[i], 64 * pair(nb, np_))
                        act.wait_ge(s_kq2[i], 32 * pair(nb, np_))
                if phase == "start" and h == 0:
                    act.wait_ge(s_ident, 4)
                act.activation(q32[:, half(h)], misc[:, k, 0:HALF], ACT.Copy)
                act.activation(hi[:, half(h)], misc[:, k, 0:HALF], ACT.Copy).then_inc(s_hi, 1)
                act.wait_ge(s_hi, 2 * pair(nb, np_) + h + 1)
                act.sem_inc(bank_free[k], 1)

            def values(phase, b, step, item, nxt):
                k, n = bank(phase, b, step, item)
                act.wait_ge(bank_full[k], n + 1)
                if phase != "start" and not (phase == "first" and step[0] == 0 and step[1] == 0):
                    act.wait_ge(s_pv, (head(*nxt) - 1) * KT)
                act.activation(val[:, nxt[2], :, :],
                               misc[:, k, :].rearrange("p (k n) -> p k n", n=P), ACT.Copy).then_inc(s_val, 1)
                act.wait_ge(s_val, head(*nxt) + 1)
                act.sem_inc(bank_free[k], 1)

            def widen(prev):
                act.wait_ge(s_rden, head(*prev, 1) + 1)
                act.wait_ge(s_cadd, pair(*prev) + 1)
                for i in range(2):
                    last = act.activation(rwide[:, :, i, :], rden[:, i, :].unsqueeze(2).to_broadcast([P, KT, DK]), ACT.Copy)
                last.then_inc(s_rwide, 1)

            def copy_context(b, p, i):
                act.wait_ge(s_pv, (head(b, p, i) + 1) * KT)
                if i == 0 and not (isinstance(b, int) and b == 0 and p == 0):
                    act.wait_ge(s_cnorm, pair(b, p))
                act.activation(ca[DK * i:DK * i + DK, :], pv[0:DK, :], ACT.Copy)
                act.activation(cb[DK * i:DK * i + DK, :], pv[DK:P, :], ACT.Copy).then_inc(s_cab, 1)

            def exponentials(b, p, i, t, first):
                n = head(b, p, i) * KT + t
                if not (first and t < NP32):
                    act.wait_ge(s_sum, 7 * head(b, p, i) + (max(t - NP32, 1) if t >= NP32 else t + NP32 - 7))
                    act.wait_ge(s_plo, n - NP32 + 1)
                    act.wait_ge(s_pv, n - NPHI + 1)
                for h in range(2):
                    act.wait_ge(s_sc, 2 * n + h + 1)
                    act.activation(p32[:, t % NP32, half(h)], sc[:, h, :], ACT.Exp, scale=SCALE).then_inc(s_p32, 1)
                    act.activation(phi[:, t % NPHI, half(h)], sc[:, h, :], ACT.Exp, scale=SCALE).then_inc(s_phi, 1)

            def do(phase, b, p, step, items, nxt):
                for item in items:
                    if item[0] == "proj":
                        high_part(phase, b, p, step, item[1])
                    elif item[0] == "vt":
                        values(phase, b, step, item, nxt)
                    elif item[0] == "drow":
                        widen(before(b, p))

            def start():
                do("start", 0, 0, "pair", PHASES["start"]["pair"], None)
                do("start", 0, 0, "head", PHASES["start"]["head"], (0, 0, 0))

            def batch(phase, b):
                for p in range(PAIRS):
                    for i in range(2):
                        for t in range(KT):
                            first = phase == "first" and p == 0 and i == 0
                            exponentials(b, p, i, t, first)
                            if t == LAG - 1 and not first:
                                copy_context(*((b, p, 0) if i == 1 else (*before(b, p), 1)))
                            do(phase, b, p, (p, i, t), PHASES[phase][(p, i, t)], following(b, p, i))

            def end():
                copy_context(B - 1, PAIRS - 1, 1)
                widen((B - 1, PAIRS - 1))

            run(act, start, batch, end)

        @block.gpsimd
        def _(pool):
            def constants():
                eye = q32[:, 0:P]
                pool.memset(eye, 0.0).then_inc(s_ident, 1)
                pool.memset(ones[:], 1.0).then_inc(s_ident, 1)
                pool.wait_ge(s_ident, 2)
                pool.affine_select(out=eye, in_=eye, compare_op=ALU.not_equal, fill=1.0, base=0,
                                   pattern=[[-1, P]], channel_multiplier=1).then_inc(s_ident, 1)
                pool.wait_ge(s_ident, 3)
                pool.tensor_copy(ident_r[:], eye).then_inc(s_ident, 1)

            def add(b, p, i, t):
                n = head(b, p, i) * KT + t
                acc = psumk[:, i, :]
                pool.wait_ge(s_p32, 2 * n + 2)
                if t == 1:
                    if not (isinstance(b, int) and b == 0 and p == 0):
                        pool.wait_ge(s_rden, head(b, p, i) - 1)
                    pool.tensor_tensor(acc, p32[:, 0, :], p32[:, 1, :], ALU.add).then_inc(s_sum, 1)
                else:
                    pool.wait_ge(s_sum, 7 * head(b, p, i) + t - 1)
                    pool.tensor_tensor(acc, acc, p32[:, t % NP32, :], ALU.add).then_inc(s_sum, 1)

            def add_parts(b, p):
                pool.wait_ge(s_cab, head(b, p, 1) + 1)
                pool.tensor_tensor(ca[:], ca[:], cb[:], ALU.add).then_inc(s_cadd, 1)

            def start():
                constants()

            def batch(phase, b):
                for p in range(PAIRS):
                    for i in range(2):
                        for t in range(1, KT):
                            first = phase == "first" and p == 0
                            add(b, p, i, t)
                            if i == 0 and t == LAG and not first:
                                add_parts(*before(b, p))

            run(pool, start, batch, lambda: add_parts(B - 1, PAIRS - 1))

        @block.vector
        def _(dve):
            def constants():
                dve.memset(keys2[DK:BAND, :, :].bitcast(F32), 0.0).then_inc(s_zero, 1)
                dve.memset(quer2[DK:BAND, :, :].bitcast(F32), 0.0).then_inc(s_zero, 1)
                dve.wait_ge(s_zero, 2)
                dve.memset(keys2[DK:DK + 2, :, :].bitcast(F32), 1.0).then_inc(s_zero, 1)

            def stage(b, p, part):
                if part == "lo":
                    dve.wait_ge(s_hi, 2 * pair(b, p) + 2)
                    dve.tensor_tensor(lo[:], q32[:], hi[:].bitcast(F32), ALU.subtract).then_inc(s_lo, 1)
                elif part == "mhi":
                    if p == 0:
                        dve.wait_ge(s_x, 32 * b + 32)
                    dve.tensor_tensor(mhi[:], hi[:].bitcast(F32), mask[:], ALU.mult)
                else:
                    dve.wait_ge(s_lo, pair(b, p) + 1)
                    dve.tensor_tensor(mlo[:], lo[:].bitcast(F32), mask[:], ALU.mult).then_inc(s_masked, 1)

            def maxima(phase, b, step, item, nxt):
                nxt = max_head(phase, item, nxt)
                k, n = bank(phase, b, step, item)
                q = item[1]
                dve.wait_ge(bank_full[k], n + 1)
                if q == 0 and not (phase == "start" and item[2] == 0):
                    dve.wait_ge(s_mneg, head(*nxt))
                reduced = dve.tensor_reduce(mrow[:, q:q + 1], misc[:, k, :], AX.X, ALU.max)
                if q < KT - 1:
                    reduced.then_inc(bank_free[k], 1)
                else:
                    reduced.then_inc(s_mrow, 1)
                    dve.wait_ge(s_mrow, head(*nxt) + 1)
                    dve.sem_inc(bank_free[k], 1)

            def max_rows(phase, b, step, item, nxt):
                g = head(*nxt)
                k, n = bank(phase, b, step, item)
                if phase != "start":
                    pb, pp, pi = (nxt[0], nxt[1], 0) if nxt[2] == 1 else (*before(nxt[0], nxt[1]), 1)
                    dve.wait_ge(s_rows[pi], 64 * (pair(pb, pp) + 1))
                if nxt[1] == 0 and nxt[2] == 0:
                    dve.wait_ge(s_mask8, 16 * nxt[0] + 16)
                    dve.tensor_copy(mparts[:, 2, :], mask8[:])
                    dve.tensor_scalar(off8[:], mask8[:], -1.0, BIG, ALU.add, ALU.mult)
                dve.wait_ge(bank_full[k], n + 1)
                dve.scalar_tensor_tensor(out=mneg[:], in0=misc[0:KT, k, 0:P], scalar=-1.0, in1=mask8[:],
                                         op0=ALU.mult, op1=ALU.mult).then_inc(s_mneg, 1)
                dve.wait_ge(s_mneg, g + 1)
                dve.sem_inc(bank_free[k], 1)
                dve.tensor_copy(mparts[:, 0, :], mneg[:]).then_inc(s_mphi, 1)
                dve.wait_ge(s_mphi, g + 1)
                dve.tensor_tensor(mparts[:, 1, :], mneg[:], mparts[:, 0, :].bitcast(F32),
                                  ALU.subtract).then_inc(s_mparts, 1)

            def denominators(phase, b, step, item, prev):
                k, n = bank(phase, b, step, item)
                dve.wait_ge(bank_full[k], n + 1)
                j = pair(prev[0], prev[1])
                if prev[2] == 0 and not (isinstance(j, int) and j == 0):
                    dve.wait_ge(s_cnorm, j)
                dve.reciprocal(rden[:, prev[2], :], misc[:, k, 0:KT]).then_inc(s_rden, 1)
                dve.wait_ge(s_rden, head(*prev) + 1)
                dve.sem_inc(bank_free[k], 1)

            def normalise(phase, b, step, item, prev):
                k, n = bank(phase, b, step, item)
                j = pair(*prev)
                dve.wait_ge(s_cadd, j + 1)
                if not (isinstance(j, int) and j == 0):
                    dve.wait_ge(s_ct, 16 * j)
                dve.wait_ge(bank_full[k], n + 1)
                dve.tensor_tensor(cnorm[:], misc[:, k, :], ca[:], ALU.mult).then_inc(s_cnorm, 1)
                dve.wait_ge(s_cnorm, j + 1)
                dve.sem_inc(bank_free[k], 1)

            def residual(phase, b, step, item, prev_b):
                k, n = bank(phase, b, step, item)
                m, h = item[1] // 2, item[1] % 2
                if h == 0:
                    dve.wait_ge(s_xo_in[m % 2], prev_b * 32 + 16 * (m // 2) + 16)
                dve.wait_ge(bank_full[k], n + 1)
                o = xo[:, m % 2, half(h)]
                dve.tensor_tensor(o, misc[:, k, 0:HALF], o, ALU.add).then_inc(s_xo, 1)
                dve.wait_ge(s_xo, prev_b * 2 * DT + item[1] + 1)
                dve.sem_inc(bank_free[k], 1)

            def split(b, p, i, t, first):
                n = head(b, p, i) * KT + t
                dve.wait_ge(s_phi, 2 * n + 2)
                if not (first and t < NPLO):
                    dve.wait_ge(s_pv, n - NPLO + 1)
                dve.tensor_tensor(plo[:, t % NPLO, :], p32[:, t % NP32, :], phi[:, t % NPHI, :].bitcast(F32),
                                  ALU.subtract).then_inc(s_plo, 1)

            def do(phase, b, p, step, items, nxt):
                for item in items:
                    if item[0] == "max":
                        maxima(phase, b, step, item, nxt)
                    elif item[0] == "mt":
                        max_rows(phase, b, step, item, nxt)
                    elif item[0] == "dcol":
                        denominators(phase, b, step, item, head_before(b, p, step[1]))
                    elif item[0] == "drow":
                        normalise(phase, b, step, item, before(b, p))
                    elif item[0] == "out":
                        residual(phase, b, step, item, b - 1)

            def start():
                constants()
                for part in STAGE_AT.values():
                    stage(0, 0, part)
                do("start", 0, 0, "head", PHASES["start"]["head"], (0, 0, 0))

            def batch(phase, b):
                for p in range(PAIRS):
                    for i in range(2):
                        for t in range(KT):
                            first = phase == "first" and p == 0 and i == 0
                            if t > 0:
                                split(b, p, i, t - 1, first)
                            elif not first:
                                hb, hp, hh = (b, p, 0) if i == 1 else (*before(b, p), 1)
                                split(hb, hp, hh, KT - 1, False)
                            do(phase, b, p, (p, i, t), PHASES[phase][(p, i, t)], following(b, p, i))
                            if i == 0 and t in STAGE_AT and not (phase == "last" and p == PAIRS - 1):
                                stage(*next_pair(b, p), STAGE_AT[t])

            def end():
                split(B - 1, PAIRS - 1, 1, KT - 1, False)
                denominators("end", B - 1, "den", ("dcol",), (B - 1, PAIRS - 1, 1))
                normalise("end", B - 1, "den", ("drow",), (B - 1, PAIRS - 1))
                for item in PHASES["end"]["out"]:
                    residual("end", B - 1, "out", item, B - 1)

            run(dve, start, batch, end)


TG = P
CH = 16
NG = P // CH
NC = D // CH
NB = 2
ROUNDS = B // NB
PER_BANK = HALF // (NB * NC)
NBANK = 8
UNITS = 8
NPART = 4
NXIN = 3
TU = TG // UNITS
FILLS = TU // PER_BANK


def build_conv(nc, x1, cond, bias, out):
    with ExitStack() as ctx:
        def sb(name, shape, dt):
            return ctx.enter_context(nc.sbuf_tensor(name, shape, dt))

        def sem(name):
            return ctx.enter_context(nc.semaphore(name))

        toep = sb("toep", [P, 2, TG, P], BF16)
        taps = sb("taps", [P, CH, TG], F32)
        keep = sb("keep", [P, 2, P], F32)
        eye = sb("eye", [P, P], F32)
        own = sb("own", [P, CH], F32)
        brow = sb("brow", [P, TG], F32)
        xin = sb("xin", [P, NXIN, NB * NC, TG], F32)
        parts = sb("parts", [P, NPART, 3, NB * NC, TU], BF16)
        acc = [ctx.enter_context(nc.psum_tensor(f"acc{k}", [P, HALF], F32)) for k in range(NBANK)]

        s_taps = sem("s_taps")
        s_keep = sem("s_keep")
        s_own = sem("s_own")
        s_toep = sem("s_toep")
        s_toep_p = sem("s_toep_p")
        s_in = [sem(f"s_in{k}") for k in range(NXIN)]
        s_p0 = sem("s_p0")
        s_r0 = sem("s_r0")
        s_p1 = sem("s_p1")
        s_p2 = sem("s_p2")
        s_bank = sem("s_bank")
        s_res = sem("s_res")
        s_out = [sem(f"s_out{k}") for k in range(NXIN)]
        block = ctx.enter_context(nc.Block())

        def rows_of(t, r, g):
            return t.rearrange("b d t -> (b d) t")[r * NB * D:(r + 1) * NB * D, g * TG:(g + 1) * TG].rearrange(
                "(c l) n -> l c n", l=CH)

        N_TAPS = 16 * (2 * CH - 1 + NG)
        LOADS = 16 * NG
        ON_DVE = 10

        @block.sync
        def _(sp):
            def load(r):
                for g in range(NG):
                    sp.dma_start(xin[g * CH:(g + 1) * CH, r % NXIN], rows_of(x1, r, g)).then_inc(s_in[r % NXIN], 16)

            def store(r):
                sp.wait_ge(s_res, UNITS * FILLS * (r + 1))
                for g in range(NG):
                    sp.dma_start(rows_of(out, r, g), xin[g * CH:(g + 1) * CH, r % NXIN]).then_inc(s_out[r % NXIN], 16)

            load(0)
            for l in range(CH):
                sp.dma_start(taps[l:P:CH, 0:CH - l, :], cond[l:CH, :].rearrange("j (g n) -> g j n", n=TG)).then_inc(s_taps, 16)
                if l:
                    sp.dma_start(taps[l:P:CH, CH - l:CH, :],
                                 cond[0:l, :].rearrange("j (g n) -> g j n", n=TG)).then_inc(s_taps, 16)
            for g in range(NG):
                b = bias[g * TG:(g + 1) * TG].rearrange("(o n) -> o n", o=1)
                sp.dma_start(brow[g * CH:(g + 1) * CH, :], b.to_broadcast([CH, TG])).then_inc(s_taps, 16)
            for r in range(1, NXIN):
                load(r)
            for r in range(ROUNDS):
                store(r)
                if r + NXIN < ROUNDS:
                    sp.wait_ge(s_out[r % NXIN], LOADS * (r // NXIN + 1))
                    load(r + NXIN)
            for r in range(ROUNDS - NXIN, ROUNDS):
                sp.wait_ge(s_out[r % NXIN], LOADS * (r // NXIN + 1))

        def matrix(w, l):
            o = toep[:, w].rearrange("p n (g l) -> p n g l", l=CH)[:, :, :, l]
            c = taps[:, CH - 1 - l, :].unsqueeze(2).to_broadcast([P, TG, NG])
            m = keep[:, w].rearrange("p (o g l) -> p o g l", o=1, l=CH)[:, :, :, l].to_broadcast([P, TG, NG])
            return o, c, m

        def unit(r, u):
            return xin[:, r % NXIN, :, u * TU:(u + 1) * TU]

        @block.gpsimd
        def _(pool):
            pool.memset(keep[:], 1.0).then_inc(s_keep, 1)
            pool.memset(eye[:], 0.0).then_inc(s_keep, 1)
            pool.wait_ge(s_keep, 2)
            m = keep[:, 0, :].rearrange("p (g l) -> p g l", l=CH)
            m1 = keep[:, 1, :].rearrange("p (g l) -> p g l", l=CH)
            pool.affine_select(out=m, in_=m, compare_op=ALU.is_ge, fill=0.0, base=0,
                               pattern=[[CH, NG], [1, CH]], channel_multiplier=-1).then_inc(s_keep, 1)
            pool.affine_select(out=m1, in_=m1, compare_op=ALU.is_ge, fill=0.0, base=-1,
                               pattern=[[-CH, NG], [-1, CH]], channel_multiplier=1).then_inc(s_keep, 1)
            pool.wait_ge(s_keep, 4)
            pool.affine_select(out=m, in_=m, compare_op=ALU.is_ge, fill=0.0, base=0,
                               pattern=[[-CH, NG], [0, CH]], channel_multiplier=1).then_inc(s_keep, 1)
            pool.affine_select(out=m1, in_=m1, compare_op=ALU.is_ge, fill=0.0, base=CH - 1,
                               pattern=[[CH, NG], [0, CH]], channel_multiplier=-1).then_inc(s_keep, 1)
            pool.affine_select(out=eye[:], in_=eye[:], compare_op=ALU.not_equal, fill=1.0, base=0,
                               pattern=[[-1, P]], channel_multiplier=1).then_inc(s_keep, 1)
            pool.wait_ge(s_keep, 7)
            pool.wait_ge(s_taps, N_TAPS)
            for l in range(ON_DVE, CH):
                o, c, m = matrix(1, l)
                pool.tensor_tensor(o, c, m, ALU.mult).then_inc(s_toep_p, 1)
            for r in range(ROUNDS):
                for u in range(UNITS):
                    pool.wait_ge(s_p0, UNITS * r + u + 1)
                    pool.tensor_tensor(unit(r, u), unit(r, u), parts[:, u % NPART, 0], ALU.subtract).then_inc(s_r0, 1)

        @block.scalar
        def _(act):
            def first_part(r, u):
                if u == 0:
                    act.wait_ge(s_in[r % NXIN], LOADS * (r // NXIN + 1))
                if UNITS * r + u >= NPART:
                    act.wait_ge(s_bank, FILLS * (UNITS * r + u + 1 - NPART))
                act.activation(parts[:, u % NPART, 0], unit(r, u), ACT.Copy).then_inc(s_p0, 1)

            def second_part(r, u):
                act.wait_ge(s_r0, UNITS * r + u + 1)
                act.activation(parts[:, u % NPART, 1], unit(r, u), ACT.Copy).then_inc(s_p1, 1)

            order = [(r, u) for r in range(ROUNDS) for u in range(UNITS)]
            first_part(*order[0])
            for k, ru in enumerate(order):
                if k + 1 < len(order):
                    first_part(*order[k + 1])
                second_part(*ru)

        @block.vector
        def _(dve):
            dve.wait_ge(s_keep, 7)
            dve.tensor_reduce(own[:], eye[:].rearrange("p (g l) -> p l g", l=CH), AX.X, ALU.max).then_inc(s_own, 1)
            dve.wait_ge(s_own, 1)
            dve.wait_ge(s_taps, N_TAPS)
            for l in range(CH):
                o, c, m = matrix(0, l)
                dve.scalar_tensor_tensor(out=o, in0=c, scalar=own[:, l:l + 1], in1=m,
                                         op0=ALU.add, op1=ALU.mult).then_inc(s_toep, 1)
            for l in range(ON_DVE):
                o, c, m = matrix(1, l)
                dve.tensor_tensor(o, c, m, ALU.mult).then_inc(s_toep, 1)

            def third_part(r, u):
                dve.wait_ge(s_p1, UNITS * r + u + 1)
                dve.tensor_tensor(parts[:, u % NPART, 2], unit(r, u), parts[:, u % NPART, 1], ALU.subtract).then_inc(s_p2, 1)

            def results(r, u):
                dve.wait_ge(s_p2, UNITS * r + u + 1)
                for f in range(FILLS):
                    n = FILLS * (UNITS * r + u) + f
                    dve.wait_ge(s_bank, n + 1)
                    tok = slice(u * TU + f * PER_BANK, u * TU + (f + 1) * PER_BANK)
                    dve.tensor_tensor(xin[:, r % NXIN, :, tok], acc[n % NBANK][:].rearrange("p (n k) -> p k n", n=PER_BANK),
                                      brow[:, tok].rearrange("p (o n) -> p o n", o=1).to_broadcast([P, NB * NC, PER_BANK]),
                                      ALU.add).then_inc(s_res, 1)

            order = [(r, u) for r in range(ROUNDS) for u in range(UNITS)]
            third_part(*order[0])
            for k, ru in enumerate(order):
                if k + 1 < len(order):
                    third_part(*order[k + 1])
                results(*ru)

        @block.tensor
        def _(pe):
            pe.wait_ge(s_toep, CH + ON_DVE)
            pe.wait_ge(s_toep_p, CH - ON_DVE)
            for r in range(ROUNDS):
                for u in range(UNITS):
                    pe.wait_ge(s_p2, UNITS * r + u + 1)
                    for f in range(FILLS):
                        at = FILLS * (UNITS * r + u) + f
                        if at >= NBANK:
                            pe.wait_ge(s_res, at + 1 - NBANK)
                        for n in range(PER_BANK):
                            k = f * PER_BANK + n
                            tok = u * TU + k
                            o = acc[at % NBANK][:, n * NB * NC:(n + 1) * NB * NC]
                            for part in range(3):
                                pe.matmul(o, toep[:, 0, tok, :], parts[:, u % NPART, part, :, k],
                                          start=(part == 0), stop=False, skip_group_check=True)
                            for part in range(3):
                                src = parts[:, u % NPART, part, :, k].rearrange("p (b c) -> p b c", b=NB)[:, :, 0:NC - 1]
                                last = pe.matmul(o.rearrange("p (b c) -> p b c", b=NB)[:, :, 1:NC], toep[:, 1, tok, :], src,
                                                 start=False, stop=(part == 2), skip_group_check=True)
                        last.then_inc(s_bank, 1)


def build(nc, x, cond, wqT, woT, bias, x1, out):
    build_attention(nc, x, cond, wqT, woT, x1)
    build_conv(nc, x1, cond, bias, out)


def kernel(x, cond_2048, L0_cond_Wq, L0_cond_Wo, L1_cond_b):
    import concourse.bacc as bacc
    from concourse.bass_utils import run_bass_kernel_spmd

    nc = bacc.Bacc("TRN2", target_bir_lowering=False, num_devices=1)
    arrays = {
        "x": np.ascontiguousarray(x),
        "cond": np.ascontiguousarray(cond_2048),
        "wqT": np.ascontiguousarray(np.asarray(L0_cond_Wq).T),
        "woT": np.ascontiguousarray(np.asarray(L0_cond_Wo).T),
        "bias": np.ascontiguousarray(L1_cond_b),
    }
    aps = [nc.dram_tensor(k, a.shape, mybir.dt.from_np(a.dtype), kind="ExternalInput").ap() for k, a in arrays.items()]
    x1 = nc.dram_tensor("x1", (B, D, T), F32, kind="Internal").ap()
    out = nc.dram_tensor("out", (B, D, T), F32, kind="ExternalOutput").ap()
    build(nc, *aps, x1, out)
    r = run_bass_kernel_spmd(nc, [arrays], core_ids=[0])
    return r.results[0]["out"]
```
